# Optimizing a Trainium2 kernel written in Bass

```python
import numpy as np
import jax
import jax.numpy as jnp

def _softmax(x, axis=-1):
    return jax.nn.softmax(x, axis=axis)

def _gelu(x):
    return jax.nn.gelu(x, approximate=True)

def _silu(x):
    return jax.nn.silu(x)

def _sigmoid(x):
    return jax.nn.sigmoid(x)

def _layernorm(x, axis=-1, eps=1e-05):
    m = jnp.mean(x, axis=axis, keepdims=True)
    v = jnp.var(x, axis=axis, keepdims=True)
    return (x - m) / jnp.sqrt(v + eps)

def _scatter_add(tgt, idx, src, axis=0):
    return tgt.at[idx].add(src)

def _segment_sum(src, seg, n):
    return jax.ops.segment_sum(src, seg, n)
kernel_name = 'mk_xattn_seq_d1_seqx_r2_4a6faf'

def setup_inputs(seed: int=0):
    np.random.seed(seed)
    _w = jnp.asarray

    def _rec_inputs():
        import jax
        import jax.numpy as jnp
        _rk = jax.random.key(seed)
        x = -1.394e-06 + 0.9999 * jax.random.normal(jax.random.fold_in(_rk, 1), (2, 2048, 512), jnp.float32)
        _lenS = 2048 - jax.random.randint(jax.random.fold_in(_rk, 7), (2,), 0, max(1, 2048 // 4) + 1, jnp.int32)
        _lenS2 = 77 - jax.random.randint(jax.random.fold_in(_rk, 8), (2,), 0, max(1, 77 // 4) + 1, jnp.int32)
        _ctx_1024P = jax.random.normal(jax.random.fold_in(_rk, 11), (2, 16, 512), jnp.float32)
        _ctx_1024c = jax.random.dirichlet(jax.random.fold_in(_rk, 511), 0.3 * jnp.ones((16,), jnp.float32), (2, 77))
        _ctx_1024t = jnp.einsum('bsk,bkd->bsd', _ctx_1024c, _ctx_1024P)
        _ctx_1024t = _ctx_1024t * jax.lax.rsqrt(jnp.mean(jnp.square(_ctx_1024t)) + 1e-12) * 0.953939
        ctx_1024 = -0.000292821 + 1.00034 * (_ctx_1024t + 0.3 * jax.random.normal(jax.random.fold_in(_rk, 611), (2, 77, 512), jnp.float32))
        return (x, ctx_1024)
    x, ctx_1024 = _rec_inputs()

    def _L0_xattn_setup():
        import jax, jax.numpy as jnp
        import numpy as np
        D, H, DFF, MD = (512, 16, 2048, 128)
        B, TS, TT = (8, 256, 256)
        EPS = 1e-06

        def _ln(x, s, b):
            m = jnp.mean(x, axis=-1, keepdims=True)
            v = jnp.mean((x - m) ** 2, axis=-1, keepdims=True)
            return (x - m) * jax.lax.rsqrt(v + EPS) * s + b

        def _rel_bias(emb, qlen, klen):
            q = jnp.arange(qlen)[:, None]
            k = jnp.arange(klen)[None, :]
            rp = k - q
            bucket = jnp.where(rp < 0, jnp.minimum(-rp, MD - 1), jnp.minimum(rp, MD - 1) + MD)
            return emb[bucket].transpose(2, 0, 1)

        def _mha(xq, xkv, w_in, b_in, w_out, b_out, bias):
            Bq, Tq, _ = xq.shape
            Tk = xkv.shape[1]
            hd = D // H
            wq, wk, wv = jnp.split(w_in, 3, axis=0)
            bq, bk, bv = jnp.split(b_in, 3, axis=0)
            q = (xq @ wq.T + bq).reshape(Bq, Tq, H, hd).transpose(0, 2, 1, 3)
            k = (xkv @ wk.T + bk).reshape(Bq, Tk, H, hd).transpose(0, 2, 1, 3)
            v = (xkv @ wv.T + bv).reshape(Bq, Tk, H, hd).transpose(0, 2, 1, 3)
            scores = jnp.einsum('bhqd,bhkd->bhqk', q, k) / jnp.sqrt(jnp.asarray(hd, xq.dtype))
            scores = scores + bias[None]
            attn = jax.nn.softmax(scores, axis=-1)
            out = jnp.einsum('bhqk,bhkd->bhqd', attn, v)
            out = out.transpose(0, 2, 1, 3).reshape(Bq, Tq, D)
            return out @ w_out.T + b_out
        key = jax.random.key(seed)
        ks = jax.random.split(key, 40)
        std = 0.02

        def n(i, shape):
            return jax.random.normal(ks[i], shape, dtype=jnp.float32) * std
        return {'src': jax.random.normal(ks[0], (B, TS, D), dtype=jnp.float32), 'tgt': jax.random.normal(ks[1], (B, TT, D), dtype=jnp.float32), 'enc_in_w': n(2, (3 * D, D)), 'enc_in_b': jnp.zeros((3 * D,)), 'enc_out_w': n(3, (D, D)), 'enc_out_b': jnp.zeros((D,)), 'enc_ff1_w': n(4, (DFF, D)), 'enc_ff1_b': jnp.zeros((DFF,)), 'enc_ff2_w': n(5, (D, DFF)), 'enc_ff2_b': jnp.zeros((D,)), 'enc_n1_s': jnp.ones((D,)), 'enc_n1_b': jnp.zeros((D,)), 'enc_n2_s': jnp.ones((D,)), 'enc_n2_b': jnp.zeros((D,)), 'enc_rel': n(6, (2 * MD, H)), 'dec_sa_in_w': n(7, (3 * D, D)), 'dec_sa_in_b': jnp.zeros((3 * D,)), 'dec_sa_out_w': n(8, (D, D)), 'dec_sa_out_b': jnp.zeros((D,)), 'dec_ca_in_w': n(9, (3 * D, D)), 'dec_ca_in_b': jnp.zeros((3 * D,)), 'dec_ca_out_w': n(10, (D, D)), 'dec_ca_out_b': jnp.zeros((D,)), 'dec_ff1_w': n(11, (DFF, D)), 'dec_ff1_b': jnp.zeros((DFF,)), 'dec_ff2_w': n(12, (D, DFF)), 'dec_ff2_b': jnp.zeros((D,)), 'dec_n1_s': jnp.ones((D,)), 'dec_n1_b': jnp.zeros((D,)), 'dec_n2_s': jnp.ones((D,)), 'dec_n2_b': jnp.zeros((D,)), 'dec_n3_s': jnp.ones((D,)), 'dec_n3_b': jnp.zeros((D,)), 'dec_rel_self': n(13, (2 * MD, H)), 'dec_rel_cross': n(14, (2 * MD, H))}
    _L0_xattn_all = _L0_xattn_setup()
    _L0_xattn_in = {k: v for k, v in _L0_xattn_all.items() if k in ('enc_in_w', 'enc_in_b', 'enc_out_w', 'enc_out_b', 'enc_ff1_w', 'enc_ff1_b', 'enc_ff2_w', 'enc_ff2_b', 'enc_n1_s', 'enc_n1_b', 'enc_n2_s', 'enc_n2_b', 'enc_rel', 'dec_sa_in_w', 'dec_sa_in_b', 'dec_sa_out_w', 'dec_sa_out_b', 'dec_ca_in_w', 'dec_ca_in_b', 'dec_ca_out_w', 'dec_ca_out_b', 'dec_ff1_w', 'dec_ff1_b', 'dec_ff2_w', 'dec_ff2_b', 'dec_n1_s', 'dec_n1_b', 'dec_n2_s', 'dec_n2_b', 'dec_n3_s', 'dec_n3_b', 'dec_rel_self', 'dec_rel_cross')}
    del _L0_xattn_all
    return {'x': x, 'ctx_1024': ctx_1024, 'L0_xattn_enc_in_w': _L0_xattn_in['enc_in_w'], 'L0_xattn_enc_in_b': _L0_xattn_in['enc_in_b'], 'L0_xattn_enc_out_w': _L0_xattn_in['enc_out_w'], 'L0_xattn_enc_out_b': _L0_xattn_in['enc_out_b'], 'L0_xattn_enc_ff1_w': _L0_xattn_in['enc_ff1_w'], 'L0_xattn_enc_ff1_b': _L0_xattn_in['enc_ff1_b'], 'L0_xattn_enc_ff2_w': _L0_xattn_in['enc_ff2_w'], 'L0_xattn_enc_ff2_b': _L0_xattn_in['enc_ff2_b'], 'L0_xattn_enc_n1_s': _L0_xattn_in['enc_n1_s'], 'L0_xattn_enc_n1_b': _L0_xattn_in['enc_n1_b'], 'L0_xattn_enc_n2_s': _L0_xattn_in['enc_n2_s'], 'L0_xattn_enc_n2_b': _L0_xattn_in['enc_n2_b'], 'L0_xattn_enc_rel': _L0_xattn_in['enc_rel'], 'L0_xattn_dec_sa_in_w': _L0_xattn_in['dec_sa_in_w'], 'L0_xattn_dec_sa_in_b': _L0_xattn_in['dec_sa_in_b'], 'L0_xattn_dec_sa_out_w': _L0_xattn_in['dec_sa_out_w'], 'L0_xattn_dec_sa_out_b': _L0_xattn_in['dec_sa_out_b'], 'L0_xattn_dec_ca_in_w': _L0_xattn_in['dec_ca_in_w'], 'L0_xattn_dec_ca_in_b': _L0_xattn_in['dec_ca_in_b'], 'L0_xattn_dec_ca_out_w': _L0_xattn_in['dec_ca_out_w'], 'L0_xattn_dec_ca_out_b': _L0_xattn_in['dec_ca_out_b'], 'L0_xattn_dec_ff1_w': _L0_xattn_in['dec_ff1_w'], 'L0_xattn_dec_ff1_b': _L0_xattn_in['dec_ff1_b'], 'L0_xattn_dec_ff2_w': _L0_xattn_in['dec_ff2_w'], 'L0_xattn_dec_ff2_b': _L0_xattn_in['dec_ff2_b'], 'L0_xattn_dec_n1_s': _L0_xattn_in['dec_n1_s'], 'L0_xattn_dec_n1_b': _L0_xattn_in['dec_n1_b'], 'L0_xattn_dec_n2_s': _L0_xattn_in['dec_n2_s'], 'L0_xattn_dec_n2_b': _L0_xattn_in['dec_n2_b'], 'L0_xattn_dec_n3_s': _L0_xattn_in['dec_n3_s'], 'L0_xattn_dec_n3_b': _L0_xattn_in['dec_n3_b'], 'L0_xattn_dec_rel_self': _L0_xattn_in['dec_rel_self'], 'L0_xattn_dec_rel_cross': _L0_xattn_in['dec_rel_cross']}

def reference(x, ctx_1024, L0_xattn_enc_in_w, L0_xattn_enc_in_b, L0_xattn_enc_out_w, L0_xattn_enc_out_b, L0_xattn_enc_ff1_w, L0_xattn_enc_ff1_b, L0_xattn_enc_ff2_w, L0_xattn_enc_ff2_b, L0_xattn_enc_n1_s, L0_xattn_enc_n1_b, L0_xattn_enc_n2_s, L0_xattn_enc_n2_b, L0_xattn_enc_rel, L0_xattn_dec_sa_in_w, L0_xattn_dec_sa_in_b, L0_xattn_dec_sa_out_w, L0_xattn_dec_sa_out_b, L0_xattn_dec_ca_in_w, L0_xattn_dec_ca_in_b, L0_xattn_dec_ca_out_w, L0_xattn_dec_ca_out_b, L0_xattn_dec_ff1_w, L0_xattn_dec_ff1_b, L0_xattn_dec_ff2_w, L0_xattn_dec_ff2_b, L0_xattn_dec_n1_s, L0_xattn_dec_n1_b, L0_xattn_dec_n2_s, L0_xattn_dec_n2_b, L0_xattn_dec_n3_s, L0_xattn_dec_n3_b, L0_xattn_dec_rel_self, L0_xattn_dec_rel_cross):
    import jax
    import jax.numpy as jnp

    def _L0_xattn_ref(src, tgt, enc_in_w, enc_in_b, enc_out_w, enc_out_b, enc_ff1_w, enc_ff1_b, enc_ff2_w, enc_ff2_b, enc_n1_s, enc_n1_b, enc_n2_s, enc_n2_b, enc_rel, dec_sa_in_w, dec_sa_in_b, dec_sa_out_w, dec_sa_out_b, dec_ca_in_w, dec_ca_in_b, dec_ca_out_w, dec_ca_out_b, dec_ff1_w, dec_ff1_b, dec_ff2_w, dec_ff2_b, dec_n1_s, dec_n1_b, dec_n2_s, dec_n2_b, dec_n3_s, dec_n3_b, dec_rel_self, dec_rel_cross):
        import jax, jax.numpy as jnp
        import numpy as np
        D, H, DFF, MD = (512, 16, 2048, 128)
        B, TS, TT = (8, 256, 256)
        EPS = 1e-06

        def _ln(x, s, b):
            m = jnp.mean(x, axis=-1, keepdims=True)
            v = jnp.mean((x - m) ** 2, axis=-1, keepdims=True)
            return (x - m) * jax.lax.rsqrt(v + EPS) * s + b

        def _rel_bias(emb, qlen, klen):
            q = jnp.arange(qlen)[:, None]
            k = jnp.arange(klen)[None, :]
            rp = k - q
            bucket = jnp.where(rp < 0, jnp.minimum(-rp, MD - 1), jnp.minimum(rp, MD - 1) + MD)
            return emb[bucket].transpose(2, 0, 1)

        def _mha(xq, xkv, w_in, b_in, w_out, b_out, bias):
            Bq, Tq, _ = xq.shape
            Tk = xkv.shape[1]
            hd = D // H
            wq, wk, wv = jnp.split(w_in, 3, axis=0)
            bq, bk, bv = jnp.split(b_in, 3, axis=0)
            q = (xq @ wq.T + bq).reshape(Bq, Tq, H, hd).transpose(0, 2, 1, 3)
            k = (xkv @ wk.T + bk).reshape(Bq, Tk, H, hd).transpose(0, 2, 1, 3)
            v = (xkv @ wv.T + bv).reshape(Bq, Tk, H, hd).transpose(0, 2, 1, 3)
            scores = jnp.einsum('bhqd,bhkd->bhqk', q, k) / jnp.sqrt(jnp.asarray(hd, xq.dtype))
            scores = scores + bias[None]
            attn = jax.nn.softmax(scores, axis=-1)
            out = jnp.einsum('bhqk,bhkd->bhqd', attn, v)
            out = out.transpose(0, 2, 1, 3).reshape(Bq, Tq, D)
            return out @ w_out.T + b_out
        Ts, Tt = (src.shape[1], tgt.shape[1])
        eb = _rel_bias(enc_rel, Ts, Ts)
        x = src
        x = x + _mha(_ln(x, enc_n1_s, enc_n1_b), _ln(x, enc_n1_s, enc_n1_b), enc_in_w, enc_in_b, enc_out_w, enc_out_b, eb)
        h = _ln(x, enc_n2_s, enc_n2_b)
        x = x + (jax.nn.relu(h @ enc_ff1_w.T + enc_ff1_b) @ enc_ff2_w.T + enc_ff2_b)
        memory = x
        causal = jnp.where(jnp.arange(Tt)[None, :] > jnp.arange(Tt)[:, None], -jnp.inf, 0.0)
        sb = _rel_bias(dec_rel_self, Tt, Tt) + causal[None]
        cb = _rel_bias(dec_rel_cross, Tt, Ts)
        y = tgt
        yn = _ln(y, dec_n1_s, dec_n1_b)
        y = y + _mha(yn, yn, dec_sa_in_w, dec_sa_in_b, dec_sa_out_w, dec_sa_out_b, sb)
        y = y + _mha(_ln(y, dec_n2_s, dec_n2_b), memory, dec_ca_in_w, dec_ca_in_b, dec_ca_out_w, dec_ca_out_b, cb)
        h = _ln(y, dec_n3_s, dec_n3_b)
        y = y + (jax.nn.relu(h @ dec_ff1_w.T + dec_ff1_b) @ dec_ff2_w.T + dec_ff2_b)
        return y
    x = _L0_xattn_ref(ctx_1024, x, L0_xattn_enc_in_w, L0_xattn_enc_in_b, L0_xattn_enc_out_w, L0_xattn_enc_out_b, L0_xattn_enc_ff1_w, L0_xattn_enc_ff1_b, L0_xattn_enc_ff2_w, L0_xattn_enc_ff2_b, L0_xattn_enc_n1_s, L0_xattn_enc_n1_b, L0_xattn_enc_n2_s, L0_xattn_enc_n2_b, L0_xattn_enc_rel, L0_xattn_dec_sa_in_w, L0_xattn_dec_sa_in_b, L0_xattn_dec_sa_out_w, L0_xattn_dec_sa_out_b, L0_xattn_dec_ca_in_w, L0_xattn_dec_ca_in_b, L0_xattn_dec_ca_out_w, L0_xattn_dec_ca_out_b, L0_xattn_dec_ff1_w, L0_xattn_dec_ff1_b, L0_xattn_dec_ff2_w, L0_xattn_dec_ff2_b, L0_xattn_dec_n1_s, L0_xattn_dec_n1_b, L0_xattn_dec_n2_s, L0_xattn_dec_n2_b, L0_xattn_dec_n3_s, L0_xattn_dec_n3_b, L0_xattn_dec_rel_self, L0_xattn_dec_rel_cross)
    return x

_drawn_inputs = setup_inputs


def setup_inputs(seed=0):
    import zlib

    import numpy as np

    out = dict(_drawn_inputs(seed))
    spreads = {'L0_xattn_enc_in_b': (0.0, 0.8),
     'L0_xattn_enc_out_b': (0.0, 0.428),
     'L0_xattn_enc_ff1_b': (0.0, 0.8),
     'L0_xattn_enc_ff2_b': (0.0, 0.388),
     'L0_xattn_enc_n1_s': (1.0, 0.6),
     'L0_xattn_enc_n1_b': (0.0, 0.8),
     'L0_xattn_enc_n2_s': (1.0, 0.6),
     'L0_xattn_enc_n2_b': (0.0, 0.8),
     'L0_xattn_dec_sa_in_b': (0.0, 0.1),
     'L0_xattn_dec_sa_out_b': (0.0, 0.1),
     'L0_xattn_dec_ca_in_b': (0.0, 0.1),
     'L0_xattn_dec_ca_out_b': (0.0, 0.1),
     'L0_xattn_dec_ff1_b': (0.0, 0.1),
     'L0_xattn_dec_ff2_b': (0.0, 0.1),
     'L0_xattn_dec_n1_s': (1.0, 0.6),
     'L0_xattn_dec_n1_b': (0.0, 0.404),
     'L0_xattn_dec_n2_s': (1.0, 0.6),
     'L0_xattn_dec_n2_b': (0.0, 2.0),
     'L0_xattn_dec_n3_s': (1.0, 0.2),
     'L0_xattn_dec_n3_b': (0.0, 0.322)}
    factors = {'L0_xattn_enc_rel': 200.0, 'L0_xattn_dec_rel_self': 64.0, 'L0_xattn_dec_rel_cross': 200.0}
    for name, (base, spread) in spreads.items():
        noise = np.random.default_rng([zlib.crc32(name.encode()), seed]).standard_normal(out[name].shape)
        drawn = base * np.exp(spread * noise) if base else spread * noise
        out[name] = jnp.asarray(drawn.astype(out[name].dtype))
    for name, factor in factors.items():
        out[name] = (out[name] * factor).astype(out[name].dtype)
    return out
```

```python
from contextlib import ExitStack

import concourse.bass as bass
from concourse import mybir

F32 = mybir.dt.float32
F32R = mybir.dt.float32r
ALU = mybir.AluOpType
ACT = mybir.ActivationFunctionType
AX_X = mybir.AxisListType.X

P = 128
B, T, S, D, H, DFF = 2, 2048, 77, 512, 16, 2048
HD = D // H
KC = D // P
FC = DFF // P
TOK = B * T
GW = 512
NG = TOK // GW
GB = T // GW
TT = GW // P
HC = P // HD
NPAIR = H // 2
KB = T // P
SP = S + 1
VW = HD + 1
QK = 3 * HD + 1
SCALE = float(HD) ** -0.5
EPS = 1e-6
NEG = -1.0e30
GL = 384
SE = B * S


class Core:

    def __init__(self, nc):
        self.nc = nc
        self.scopes = []

    def __enter__(self):
        self.scopes.append((ExitStack(), ExitStack(), []))
        return self

    def __exit__(self, *e):
        memory, block, sems = self.scopes.pop()
        block.close()
        if sems:
            with self.nc.Block() as clearing:
                @clearing.sync
                def _(sp):
                    for sem in sems:
                        sp.sem_clear(sem)
        memory.close()

    def sb(self, name, shape, dt=F32):
        return self.scopes[-1][0].enter_context(self.nc.sbuf_tensor(name, shape, dt))

    def ps(self, name, shape):
        return self.scopes[-1][0].enter_context(self.nc.psum_tensor(name, shape, F32))

    def sem(self, name):
        self.scopes[-1][2].append(self.scopes[-1][0].enter_context(self.nc.semaphore(name)))
        return self.scopes[-1][2][-1]

    def sems(self, prefix, names):
        return {n: self.sem(f"{prefix}_{n}") for n in names.split()}

    def block(self):
        return self.scopes[-1][1].enter_context(self.nc.Block())


def raw(ap):
    return ap.bitcast(F32)


def product(pe, out, terms):
    n = 3 * len(terms)
    k = 0
    for (sh, sl), (mh, ml) in terms:
        for s, m in ((sh, mh), (sh, ml), (sl, mh)):
            last = pe.matmul(out, s, m, start=(k == 0), stop=(k == n - 1))
            k += 1
    return last


def waits(engine, sem, value):
    if not (isinstance(value, int) and value <= 0):
        engine.wait_ge(sem, value)


def encoder(k, io, dr, ident, identr, weights):
    nc = k.nc
    with k:
        xT = k.sb("enc_xT", [P, KC, SE])
        wqkv = k.sb("enc_wqkv", [P, KC, 3 * D])
        wff1 = k.sb("enc_wff1", [P, KC, DFF])
        wff2 = k.sb("enc_wff2", [P, FC, D])
        wkv, wo = wqkv[:, :, 0:2 * D], wqkv[:, :, 2 * D:3 * D]
        cols = k.sb("enc_cols", [P, io["enc_cols"].shape[1]])
        vrow = k.sb("enc_vrow", [S, 2, D])
        bias = k.sb("enc_bias", [S, HC, KC, S])
        G = k.sb("rel_rows", [H, 5, GL])
        far_sa = k.sb("rel_far_sa", [H, 1])
        far_ca = k.sb("rel_far_ca", [H, 1])
        ones = k.sb("enc_ones", [P, P])
        xc = k.sb("enc_xc", [P, KC, SE])
        sq = k.sb("enc_sq", [P, KC, SE])
        sd = k.sb("enc_sd", [P, SE])
        rs = k.sb("enc_rs", [P, SE])
        hT = k.sb("enc_hT", [P, KC, SE])
        qk = k.sb("enc_qk", [P, 2 * KC, SE])
        v = k.sb("enc_v", [S, B, D])
        sc = k.sb("enc_sc", [S, H, S])
        mx = k.sb("enc_mx", [S, H])
        den = k.sb("enc_den", [S, H])
        rden = k.sb("enc_rden", [S, H])
        prT = k.sb("enc_prT", [S, HC, KC, S])
        oT = k.sb("enc_oT", [P, KC, B, S])
        x1 = k.sb("enc_x1", [P, KC, SE])
        hid = k.sb("enc_hid", [P, FC, SE])
        mem = xc
        ckh = k.sb("enc_ckh", [P, KC, SE], F32R)
        ckl = k.sb("enc_ckl", [P, KC, SE], F32R)
        cv = sc[:].rearrange("p h k -> p (h k)")[:, 0:B * H * VW].rearrange("p (b h e) -> p b h e", b=B, h=H)
        ring = [k.ps(f"enc_ring{i}", [P, 512]) for i in range(4)]
        head = [k.ps(f"enc_head{i}", [P, KC, P]) for i in range(4)]
        s = k.sems("enc", "x wqkv wo wff1 wff2 wkv cols vrow grow gx0 gx1 g gs bias gx ones idz id idr mm xc"
                          " sq var sd rs hs h qk v st sc mx sub ex sum rec nrm pt ptc ot otc x1 hid mem ck cl cv one out")
        N1S, N1B, N2S, N2B, BQK = 0, KC, 2 * KC, 3 * KC, 4 * KC
        BO = BQK + 2 * KC
        BF1 = BO + KC
        BF2 = BF1 + FC
        BCK = BF2 + KC

        UNITS = ([("mean", 0), ("var", 0)] + [("qk", m) for m in range(2 * KC)] + [("v", b) for b in range(B)]
                 + [("att", b) for b in range(B)] + [("o", m) for m in range(KC)] + [("mean", 1), ("var", 1)]
                 + [("ff1", m) for m in range(FC)] + [("ff2", m) for m in range(KC)]
                 + [("ck", m) for m in range(KC)] + [("cv", b) for b in range(B)])

        def emptied(kind, m):
            name = {"mean": "xc", "att": "otc", "o": "x1", "ff1": "hid", "ff2": "mem", "ck": "cl"}.get(kind, kind)
            return s[name], (KC if kind == "mean" else 1) * (m + 1)

        block = k.block()

        @block.sync
        def _(sp):
            sp.dma_start(xT[:], io["ctxT"]).then_inc(s["x"], 16)
            sp.dma_start(cols[:], io["enc_cols"]).then_inc(s["cols"], 16)
            sp.dma_start(G[:], io["rel_rows"]).then_inc(s["grow"], 16)
            sp.dma_start(wqkv[:], io["enc_wqkv"]).then_inc(s["wqkv"], 16)
            sp.wait_ge(s["g"], 2)
            sp.dma_start(dr["rows"].ap(), G[:]).then_inc(s["gs"], 16)
            sp.dma_start(vrow[:], io["enc_vrow"].partition_broadcast(S)).then_inc(s["vrow"], 16)
            sp.wait_ge(s["gs"], 16)
            W = 5 * GL
            sp.dma_start(dr["en_B"].ap(), bass.AP(dr["rows"], 4 * GL + S - 1, [[W, H], [-1, S], [1, S]])).then_inc(s["gs"], 16)
            sp.wait_ge(s["gs"], 32)
            for j in range(HC):
                sp.dma_start(bias[:, j, :, :],
                             dr["en_B"].ap().rearrange("(c j) p k -> j p c k", j=HC)[j]).then_inc(s["bias"], 16)
            sp.dma_start(wff1[:], io["enc_wff1"]).then_inc(s["wff1"], 16)
            sp.wait_ge(s["v"], B)
            sp.dma_start(wo, io["enc_wo"]).then_inc(s["wo"], 16)
            sp.dma_start(wff2[:], io["enc_wff2"]).then_inc(s["wff2"], 16)
            sp.dma_start(wkv, io["enc_wkv"]).then_inc(s["wkv"], 16)
            sp.dma_start(dr["sa_T"].ap(), bass.AP(dr["rows"], P - 1, [[W, H], [-1, P], [1, 2 * P]])).then_inc(s["gx"], 16)
            sp.dma_start(dr["sa_U"].ap(), bass.AP(dr["rows"], GL + P - 1, [[W, H], [-1, P], [1, 2 * P]])).then_inc(s["gx"], 16)
            sp.dma_start(dr["ca_T"].ap(), bass.AP(dr["rows"], 2 * GL + S - 1, [[W, H], [-1, S], [1, 2 * P]])).then_inc(s["gx"], 16)
            sp.dma_start(dr["ca_U"].ap(), bass.AP(dr["rows"], 3 * GL + 2 * P - 1, [[W, H], [-1, 2 * P], [1, S]])).then_inc(s["gx"], 16)
            sp.wait_ge(s["cl"], KC)
            for b in range(B):
                for hl, t in enumerate((ckh, ckl)):
                    sp.dma_start(dr["ck"].ap()[b, hl].rearrange("(c p) t -> p c t", p=P),
                                 raw(t[:, :, b * S:(b + 1) * S])).then_inc(s["out"], 16)
            sp.wait_ge(s["cv"], B)
            for b in range(B):
                sp.dma_start(dr["cv"].ap()[:, b].rearrange("a p e -> p a e"),
                             cv[:, b].rearrange("p (a h) e -> p a (h e)", a=NPAIR)).then_inc(s["out"], 16)
            sp.wait_ge(s["gx"], 64)
            sp.wait_ge(s["out"], 16 * 3 * B)

        @block.gpsimd
        def _(pool):
            pool.memset(ident[:], 0.0).then_inc(s["idz"], 1)
            pool.wait_ge(s["idz"], 1)
            pool.affine_select(out=ident[:], in_=ident[:], compare_op=ALU.not_equal, fill=1.0, base=0,
                               pattern=[[-1, P]], channel_multiplier=1).then_inc(s["id"], 1)
            pool.wait_ge(s["wkv"], 16)
            weights.run(pool)

        @block.tensor
        def _(pe):
            def summed(out, x):
                for c in range(KC):
                    last = pe.matmul(out[:, 0:SE], ones[:], x[:, c, :], start=(c == 0), stop=(c == KC - 1))
                return last

            def projected(out, w, m, x, n=KC):
                for c in range(n):
                    last = pe.matmul(out[:, 0:SE], w[:, c, m * P:(m + 1) * P], x[:, c, :],
                                     start=(c == 0), stop=(c == n - 1))
                return last

            for n, (kind, m) in enumerate(UNITS):
                if n >= 4:
                    pe.wait_ge(*emptied(*UNITS[n - 4]))
                out = ring[n % 4]
                if kind == "mean":
                    pe.wait_ge(s["ones"], 1)
                    pe.wait_ge(s["x"], 16) if m == 0 else pe.wait_ge(s["x1"], KC)
                    last = summed(out, xT if m == 0 else x1)
                elif kind == "var":
                    pe.wait_ge(s["sq"], m + 1)
                    last = summed(out, sq)
                elif kind == "qk":
                    pe.wait_ge(s["wqkv"], 16)
                    pe.wait_ge(s["h"], KC)
                    last = projected(out, wqkv, m, hT)
                elif kind == "v":
                    for c in range(KC):
                        last = pe.matmul(out[0:S, :], hT[:, c, m * S:(m + 1) * S], wqkv[:, c, 2 * D:3 * D],
                                         start=(c == 0), stop=(c == KC - 1))
                elif kind == "att":
                    if m == 0:
                        pe.wait_ge(s["qk"], 2 * KC)
                        pe.wait_ge(s["id"], 1)
                    else:
                        pe.wait_ge(s["ptc"], HC * m)
                    for j in range(HC):
                        rows = slice(j * HD, (j + 1) * HD)
                        for c in range(KC):
                            last = pe.matmul(head[j][0:S, c, 0:S], qk[rows, c, m * S:(m + 1) * S],
                                             qk[rows, KC + c, m * S:(m + 1) * S], start=True, stop=True)
                    last.then_inc(s["st"], 1)
                    pe.wait_ge(s["nrm"], m + 1)
                    for j in range(HC):
                        for c in range(KC):
                            last = pe.transpose(head[j][0:S, c, 0:S], sc[:, j * KC + c, :], ident[0:S, 0:S])
                    last.then_inc(s["pt"], 1)
                    pe.wait_ge(s["ptc"], HC * (m + 1))
                    pe.wait_ge(s["v"], B)
                    for j in range(HC):
                        for c in range(KC):
                            h = c * HC + j
                            last = pe.matmul(out[j * HD:(j + 1) * HD, c * S:(c + 1) * S],
                                             v[:, m, h * HD:(h + 1) * HD], prT[:, j, c, :], start=True, stop=True)
                elif kind == "o":
                    pe.wait_ge(s["wo"], 16)
                    pe.wait_ge(s["otc"], B)
                    last = projected(out, wo, m, oT[:].rearrange("p c b t -> p c (b t)"))
                elif kind == "ff1":
                    pe.wait_ge(s["wff1"], 16)
                    pe.wait_ge(s["h"], 2 * KC)
                    last = projected(out, wff1, m, hT)
                elif kind == "ff2":
                    pe.wait_ge(s["wff2"], 16)
                    pe.wait_ge(s["hid"], FC)
                    last = projected(out, wff2, m, hid, FC)
                elif kind == "ck":
                    pe.wait_ge(s["wkv"], 16)
                    pe.wait_ge(s["mem"], KC)
                    last = projected(out, wkv, m, mem)
                else:
                    for c in range(KC):
                        last = pe.matmul(out[0:S, :], mem[:, c, m * S:(m + 1) * S], wkv[:, c, D:2 * D],
                                         start=(c == 0), stop=(c == KC - 1))
                last.then_inc(s["mm"], 1)

        @block.scalar
        def _(act):
            def square_root(n):
                act.wait_ge(s["xc"], KC * (n + 1))
                act.activation(sq[:], xc[:], ACT.Square).then_inc(s["sq"], 1)
                act.wait_ge(s["var"], n + 1)
                act.activation(sd[:], sd[:], ACT.Sqrt).then_inc(s["sd"], 1)

            act.wait_ge(s["id"], 1)
            act.activation(identr[:], ident[:], ACT.Copy).then_inc(s["idr"], 1)
            square_root(0)
            for b in range(B):
                act.wait_ge(s["sub"], b + 1)
                act.activation(sc[:], sc[:], ACT.Exp).then_inc(s["ex"], 1)
            square_root(1)

        @block.vector
        def _(dve):
            dve.memset(ones[:], 1.0 / D).then_inc(s["ones"], 1)
            dve.wait_ge(s["grow"], 16)
            dve.tensor_copy(far_sa[:], G[:, 0, 2 * P + P - 2:2 * P + P - 1]).then_inc(s["gx0"], 1)
            dve.tensor_copy(far_ca[:], G[:, 2, 2 * P + S - 2:2 * P + S - 1]).then_inc(s["gx0"], 1)

            def ready(n):
                dve.wait_ge(s["mm"], n + 1)

            dve.wait_ge(s["gx0"], 2)
            for i, f in ((0, far_sa), (1, far_sa), (2, far_ca), (3, far_ca)):
                dve.tensor_scalar(G[:, i, :], G[:, i, :], f[:, 0:1], 1.0 / SCALE, ALU.subtract, ALU.mult).then_inc(s["gx1"], 1)
            dve.wait_ge(s["gx1"], 4)
            dve.memset(G[:, 0, 0:P - 1], NEG).then_inc(s["g"], 1)
            dve.memset(G[:, 1, 2 * P:GL], NEG).then_inc(s["g"], 1)
            dve.wait_ge(s["cols"], 16)
            for n, (kind, m) in enumerate(UNITS):
                out = ring[n % 4]
                if kind == "mean":
                    ready(n)
                    x = xT if m == 0 else x1
                    for c in range(KC):
                        ins = dve.tensor_tensor(xc[:, c, :], x[:, c, :], out[:, 0:SE], ALU.subtract)
                        ins.then_inc(s["xc"], 1)
                elif kind == "var":
                    ready(n)
                    dve.tensor_scalar(sd[:], out[:, 0:SE], EPS, None, ALU.add).then_inc(s["var"], 1)
                    dve.wait_ge(s["sd"], m + 1)
                    dve.reciprocal(rs[:], sd[:]).then_inc(s["rs"], 1)
                    dve.wait_ge(s["rs"], m + 1)
                    sc0, bi0 = (N1S, N1B) if m == 0 else (N2S, N2B)
                    for c in range(KC):
                        dve.scalar_tensor_tensor(xc[:, c, :], xc[:, c, :], cols[:, sc0 + c:sc0 + c + 1], rs[:],
                                                 ALU.mult, ALU.mult).then_inc(s["hs"], 1)
                    dve.wait_ge(s["hs"], KC * (m + 1))
                    for c in range(KC):
                        dve.tensor_scalar(hT[:, c, :], xc[:, c, :], cols[:, bi0 + c:bi0 + c + 1], None,
                                          ALU.add).then_inc(s["h"], 1)
                elif kind == "qk":
                    ready(n)
                    dve.tensor_scalar(qk[:, m, :], out[:, 0:SE], cols[:, BQK + m:BQK + m + 1], None,
                                      ALU.add).then_inc(s["qk"], 1)
                elif kind == "v":
                    ready(n)
                    dve.wait_ge(s["vrow"], 16)
                    dve.tensor_tensor(v[:, m, :], out[0:S, :], vrow[:, 0, :], ALU.add).then_inc(s["v"], 1)
                elif kind == "att":
                    dve.wait_ge(s["st"], m + 1)
                    dve.wait_ge(s["bias"], 16 * HC)
                    for j in range(HC):
                        dve.scalar_tensor_tensor(sc[:, j * KC:(j + 1) * KC, :], head[j][0:S, :, 0:S], SCALE,
                                                 bias[:, j, :, :], ALU.mult, ALU.add).then_inc(s["sc"], 1)
                    dve.wait_ge(s["sc"], HC * (m + 1))
                    dve.tensor_reduce(mx[:], sc[:], AX_X, ALU.max).then_inc(s["mx"], 1)
                    dve.wait_ge(s["mx"], m + 1)
                    dve.tensor_tensor(sc[:], sc[:], mx[:].unsqueeze(2).to_broadcast([S, H, S]),
                                      ALU.subtract).then_inc(s["sub"], 1)
                    dve.wait_ge(s["ex"], m + 1)
                    dve.tensor_reduce(den[:], sc[:], AX_X, ALU.add).then_inc(s["sum"], 1)
                    dve.wait_ge(s["sum"], m + 1)
                    dve.reciprocal(rden[:], den[:]).then_inc(s["rec"], 1)
                    dve.wait_ge(s["rec"], m + 1)
                    dve.tensor_tensor(sc[:], sc[:], rden[:].unsqueeze(2).to_broadcast([S, H, S]),
                                      ALU.mult).then_inc(s["nrm"], 1)
                    dve.wait_ge(s["pt"], m + 1)
                    for j in range(HC):
                        dve.tensor_copy(prT[:, j, :, :], head[j][0:S, :, 0:S]).then_inc(s["ptc"], 1)
                    ready(n)
                    dve.tensor_copy(oT[:, :, m, :], out[:, 0:KC * S].rearrange("p (c t) -> p c t", c=KC))\
                       .then_inc(s["otc"], 1)
                elif kind == "o":
                    ready(n)
                    dve.scalar_tensor_tensor(x1[:, m, :], out[:, 0:SE], cols[:, BO + m:BO + m + 1], xT[:, m, :],
                                             ALU.add, ALU.add).then_inc(s["x1"], 1)
                elif kind == "ff1":
                    ready(n)
                    dve.tensor_scalar(hid[:, m, :], out[:, 0:SE], cols[:, BF1 + m:BF1 + m + 1], 0.0,
                                      ALU.add, ALU.max).then_inc(s["hid"], 1)
                elif kind == "ff2":
                    ready(n)
                    dve.scalar_tensor_tensor(mem[:, m, :], out[:, 0:SE], cols[:, BF2 + m:BF2 + m + 1], x1[:, m, :],
                                             ALU.add, ALU.add).then_inc(s["mem"], 1)
                elif kind == "ck":
                    ready(n)
                    bk = cols[:, BCK + m:BCK + m + 1]
                    dve.tensor_scalar(ckh[:, m, :], out[:, 0:SE], bk, None, ALU.add).then_inc(s["ck"], 1)
                    dve.wait_ge(s["ck"], m + 1)
                    dve.scalar_tensor_tensor(ckl[:, m, :], out[:, 0:SE], bk, raw(ckh[:, m, :]),
                                             ALU.add, ALU.subtract).then_inc(s["cl"], 1)
                else:
                    ready(n)
                    if m == 0:
                        dve.memset(cv[:, :, :, HD:VW], 1.0).then_inc(s["one"], 1)
                    dve.wait_ge(s["one"], 1)
                    dve.tensor_tensor(cv[:, m, :, 0:HD], out[0:S, :].rearrange("p (h d) -> p h d", h=H),
                                      vrow[:, 1, :].rearrange("p (h d) -> p h d", h=H), ALU.add).then_inc(s["cv"], 1)


class SplitWeights:

    def __init__(self, k, name, jobs, step):
        self.jobs, self.step = jobs, step
        self.stage = k.sb(f"{name}_stage", [P, 2, step])
        self.s = k.sems(name, "in0 in1 hi lo")

    def load(self, sp, n):
        if n >= 2:
            sp.wait_ge(self.s["lo"], n - 1)
        sp.dma_start(self.stage[:, n % 2, :], self.jobs[n][0]).then_inc(self.s[f"in{n % 2}"], 16)

    def split(self, eng, n):
        _, hi, lo = self.jobs[n]
        eng.wait_ge(self.s[f"in{n % 2}"], 16 * (n // 2 + 1))
        eng.tensor_copy(hi, self.stage[:, n % 2, :]).then_inc(self.s["hi"], 1)
        eng.wait_ge(self.s["hi"], n + 1)
        eng.tensor_tensor(lo, self.stage[:, n % 2, :], raw(hi), ALU.subtract).then_inc(self.s["lo"], 1)


    def run(self, pool):
        for n in range(len(self.jobs)):
            self.load(pool, n)
            if n:
                self.split(pool, n - 1)
        self.split(pool, len(self.jobs) - 1)


class Norm:

    def __init__(self, k, name, sb_cols, ident):
        self.ident, self.cols = ident, sb_cols
        self.stat6 = k.sb(f"{name}_stat6", [P, TT, 6])
        self.mv = k.sb(f"{name}_mv", [P, TT, 2])
        self.std = k.sb(f"{name}_std", [P, TT])
        self.rstd = k.sb(f"{name}_rstd", [P, TT])
        self.xn = k.sb(f"{name}_xn", [P, TT, D])
        self.xf = k.sb(f"{name}_xf", [P, 2, GW])
        self.hi = k.sb(f"{name}_hi", [P, 2, KC, GW], F32R)
        self.lo = k.sb(f"{name}_lo", [P, 2, KC, GW], F32R)
        self.tp = [k.ps(f"{name}_tp{i}", [P, GW]) for i in range(2)]
        self.s = k.sems(name, "stat counted aggr eps std rstd normed turned scaled hi low")

    def start(self, pe):
        pe.sem_inc(self.s["scaled"], 1)
        pe.sem_inc(self.s["low"], 1)

    def stats(self, dve, x, i):
        dve.bn_stats(self.stat6[:, i, :], x[:, i, :]).then_inc(self.s["stat"], 1)

    def normalise(self, dve, g, x, counted=False):
        s = self.s
        if not counted:
            for i in range(TT):
                self.stats(dve, x, i)
        dve.wait_ge(s["stat"], TT * g + TT)
        dve.sem_inc(s["counted"], 1)
        for i in range(TT):
            dve.bn_aggr(self.mv[:, i, :], self.stat6[:, i, :]).then_inc(s["aggr"], 1)
        dve.wait_ge(s["aggr"], TT * g + TT)
        dve.tensor_scalar(self.std[:], self.mv[:, :, 1], EPS, None, ALU.add).then_inc(s["eps"], 1)
        dve.wait_ge(s["std"], g.n + 1)
        dve.reciprocal(self.rstd[:], self.std[:]).then_inc(s["rstd"], 1)
        dve.wait_ge(s["rstd"], g.n + 1)
        waits(dve, s["turned"], KC * g)
        for i in range(TT):
            dve.tensor_scalar(self.xn[:, i, :], x[:, i, :], self.mv[:, i, 0:1], self.rstd[:, i:i + 1],
                              ALU.subtract, ALU.mult).then_inc(s["normed"], 1)

    def root(self, act, g):
        act.wait_ge(self.s["eps"], g.n + 1)
        act.activation(self.std[:], self.std[:], ACT.Sqrt).then_inc(self.s["std"], 1)

    def transpose(self, pe, g, chunks=range(KC)):
        s = self.s
        if chunks[0] == 0:
            pe.wait_ge(s["normed"], TT * g + TT)
        for c in chunks:
            waits(pe, s["scaled"], KC * g + c)
            for i in range(TT):
                last = pe.transpose(self.tp[c % 2][:, i * P:(i + 1) * P], self.xn[:, i, c * P:(c + 1) * P], self.ident[:])
            last.then_inc(s["turned"], 1)

    def scale(self, act, g, par, used):
        s = self.s
        for c in range(KC):
            act.wait_ge(s["turned"], KC * g + c + 1)
            waits(act, s["low"], KC * g + c)
            act.activation(self.xf[:, c % 2, :], self.tp[c % 2][:], ACT.Identity, bias=self.cols[:, 1, c:c + 1],
                           scale=self.cols[:, 0, c:c + 1]).then_inc(s["scaled"], 1)
            act.wait_ge(s["scaled"], KC * g + c + 2)
            if c == 0:
                waits(act, *used)
            act.activation(self.hi[:, par, c, :], self.xf[:, c % 2, :], ACT.Copy).then_inc(s["hi"], 1)

    def low(self, dve, g, par):
        s = self.s
        for c in range(KC):
            dve.wait_ge(s["hi"], KC * g + c + 1)
            dve.tensor_tensor(self.lo[:, par, c, :], self.xf[:, c % 2, :], raw(self.hi[:, par, c, :]),
                              ALU.subtract).then_inc(s["low"], 1)

    def wait_ready(self, pe, g):
        pe.wait_ge(self.s["low"], KC * g + KC + 1)

    def pair(self, par, c, cols=slice(None)):
        return self.hi[:, par, c, cols], self.lo[:, par, c, cols]


class Step:

    def __init__(self, t, i, unroll=2, nbuf=2):
        self.t, self.i, self.unroll, self.nbuf = t, i, unroll, nbuf

    def __add__(self, k):
        return Step(self.t, self.i + k, self.unroll, self.nbuf)

    @property
    def n(self):
        return self.t * self.unroll + self.i

    def __rmul__(self, k):
        return self.t * (self.unroll * k) + self.i * k

    @property
    def par(self):
        return self.i % self.nbuf

    @property
    def uses(self):
        return self.t * (self.unroll // self.nbuf) + self.i // self.nbuf

    def cols(self, width):
        start = self.t * (self.unroll * width) + self.i * width
        return slice(start, start + width) if isinstance(start, int) else bass.ds(start, width)


def run(engine, count, slot, unroll=2, nbuf=2, tail=1):
    blocks = count // unroll
    for i in range(unroll):
        slot(Step(0, i, unroll, nbuf), tail * unroll)
    with engine.Fori(1, blocks - tail) as t:
        for i in range(unroll):
            slot(Step(t, i, unroll, nbuf), tail * unroll)
    for t in range(blocks - tail, blocks):
        for i in range(unroll):
            slot(Step(t, i, unroll, nbuf), count - 1 - t * unroll - i)


def decoder_qkv(k, io, dr, ident, w):
    nc = k.nc
    NM = 2 * KC + TT
    with k:
        wh, wl = w
        lncols = k.sb("qkv_lncols", [P, 2, KC])
        bcol = k.sb("qkv_bcol", [P, 2 * KC])
        bvrow = k.sb("qkv_bvrow", [P, D])
        x = k.sb("qkv_x", [P, 2, TT, D])
        qst = k.sb("qkv_qst", [P, 4, 2, GW], F32R)
        vst = k.sb("qkv_vst", [P, 2, NPAIR, TT, 2, VW])
        ring = [k.ps(f"qkv_ring{i}", [P, GW]) for i in range(4)]
        norm = Norm(k, "ln1", lncols, ident)
        s = k.sems("qkv", "cols x0 x1 mm hi ev one q0 q1 q2 q3 v0 v1")
        block = k.block()

        @block.sync
        def _(sp):
            def load_x(g):
                waits(sp, norm.s["normed"], TT * g - TT)
                sp.dma_start(x[:, g.par], io["x"][:, g.cols(TT), :]).then_inc(s[f"x{g.par}"], 16)

            load_x(Step(0, 0))
            sp.dma_start(lncols[:], io["ln1"]).then_inc(s["cols"], 16)
            sp.dma_start(bcol[:], io["sa_bqk"]).then_inc(s["cols"], 16)
            sp.dma_start(bvrow[:], io["sa_bv"].partition_broadcast(P)).then_inc(s["cols"], 16)
            load_x(Step(0, 1))

            def slot(g, left):
                if left >= 2:
                    load_x(g + 2)
                for m in range(2 * KC):
                    sp.wait_ge(s["ev"], NM * g + m + 4)
                    c = m % KC
                    dst = dr["qk"][m // KC]
                    sp.dma_start(dst[:, c * P:(c + 1) * P, g.cols(GW)].rearrange("l p t -> p l t"),
                                 raw(qst[:, m % 4])).then_inc(s[f"q{m % 4}"], 16)
                sp.wait_ge(s["ev"], NM * g + NM + 3)
                sp.dma_start(dr["v"][:, :, g.cols(TT), :].rearrange("a p k e -> p a k e"),
                             vst[:, g.par].rearrange("p a k h e -> p a k (h e)")).then_inc(s[f"v{g.par}"], 16)
            run(sp, NG, slot)
            for n in range(4):
                sp.wait_ge(s[f"q{n}"], 16 * 2 * NG)
            for n in range(2):
                sp.wait_ge(s[f"v{n}"], 16 * NG // 2)

        @block.tensor
        def _(pe):
            norm.start(pe)
            pe.sem_inc(s["ev"], 3)
            norm.transpose(pe, Step(0, 0))

            def slot(g, left):
                norm.wait_ready(pe, g)
                for m in range(NM):
                    if m in (4, 5) and left:
                        norm.transpose(pe, g + 1, range(KC // 2 * (m - 4), KC // 2 * (m - 3)))
                    waits(pe, s["ev"], NM * g + m)
                    if m < 2 * KC:
                        terms = [((wh[:, c, m * P:(m + 1) * P], wl[:, c, m * P:(m + 1) * P]), norm.pair(g.par, c))
                                 for c in range(KC)]
                    else:
                        t = slice((m - 2 * KC) * P, (m - 2 * KC + 1) * P)
                        terms = [(norm.pair(g.par, c, t), (wh[:, c, 2 * D:], wl[:, c, 2 * D:])) for c in range(KC)]
                    mm = product(pe, ring[m % 4][:], terms)
                    mm.then_inc(s["mm"], 1)
            run(pe, NG, slot)

        @block.scalar
        def _(act):
            act.wait_ge(s["cols"], 48)
            norm.root(act, Step(0, 0))
            norm.scale(act, Step(0, 0), 0, (s["mm"], 0))

            def slot(g, left):
                if left:
                    norm.root(act, g + 1)
                for m in range(2 * KC):
                    if m == 4 and left:
                        norm.scale(act, g + 1, 1 - g.par, (s["mm"], NM * g))
                    act.wait_ge(s["mm"], NM * g + m + 1)
                    waits(act, s[f"q{m % 4}"], 16 * (2 * g + m // 4))
                    act.activation(qst[:, m % 4, 0, :], ring[m % 4][:], ACT.Identity,
                                   bias=bcol[:, m:m + 1]).then_inc(s["hi"], 1)
            run(act, NG, slot)

        @block.vector
        def _(dve):
            dve.memset(vst[:, :, :, :, :, HD:VW].rearrange("p a b c d e -> p (a b c d e)"), 1.0).then_inc(s["one"], 1)
            dve.wait_ge(s["x0"], 16)
            norm.normalise(dve, Step(0, 0), x[:, 0])
            norm.low(dve, Step(0, 0), 0)
            dve.wait_ge(s["cols"], 48)
            dve.wait_ge(s["one"], 1)

            def slot(g, left):
                if left:
                    dve.wait_ge(s[f"x{1 - g.par}"], 16 * (g + 1).uses + 16)
                    norm.normalise(dve, g + 1, x[:, 1 - g.par])
                for m in range(NM):
                    if m == 4 and left:
                        norm.low(dve, g + 1, 1 - g.par)
                    out = ring[m % 4]
                    if m < 2 * KC:
                        dve.wait_ge(s["hi"], 2 * KC * g + m + 1)
                        dve.scalar_tensor_tensor(qst[:, m % 4, 1, :], out[:], bcol[:, m:m + 1],
                                                 raw(qst[:, m % 4, 0, :]), ALU.add, ALU.subtract).then_inc(s["ev"], 1)
                    else:
                        i = m - 2 * KC
                        dve.wait_ge(s["mm"], NM * g + m + 1)
                        if i == 0:
                            waits(dve, s[f"v{g.par}"], 16 * g.uses)
                        dve.tensor_tensor(vst[:, g.par, :, i, :, 0:HD], out[:].rearrange("p (a h d) -> p a h d", a=NPAIR, h=2),
                                          bvrow[:].rearrange("p (a h d) -> p a h d", a=NPAIR, h=2), ALU.add)\
                           .then_inc(s["ev"], 1)
            run(dve, NG, slot)


def units_of(causal):
    out = []
    for g in range(GB):
        for kb in range(TT * (g + 1) if causal else 1):
            i = kb - TT * g
            if causal:
                c0 = max(0, i * P)
                bias = (min(2 * P, GW - c0), 0) if i >= 0 else (P, P) if i == -1 else (0, 0)
            else:
                c0, bias = 0, (2 * P, 0) if g == 0 else (0, 0)
            out.append((g, kb, c0, *bias))
    if not causal:
        return out
    diagonal = [[u for u in out if u[0] == g and u[1] >= TT * g] for g in range(GB)]
    whole = [[u for u in out if u[0] == g and u[1] < TT * g] for g in range(GB)]
    mixed = []
    for g in range(GB):
        if g + 1 < GB:
            mixed += whole[g][TT:]
            for a, b in zip(diagonal[g], whole[g + 1]):
                mixed += [a, b]
        else:
            rest = whole[g][TT:]
            mixed += rest[:len(rest) - TT]
            for a, b in zip(reversed(diagonal[g]), rest[len(rest) - TT:]):
                mixed += [a, b]
    assert sorted(mixed) == sorted(out)
    return mixed


TURN = (None, None)
TURN_AFTER = 2


def max_steps_of(causal):
    out = []
    if causal:
        for half, h in ((0, 0), (0, 1), (1, 0), (1, 1)):
            for qb in range(half * KB // 2, (half + 1) * KB // 2):
                end, chunk = (qb + 1) * P, 0
                while end > 0:
                    k0 = max(0, end - 512)
                    if k0 == P:
                        k0 = 2 * P
                    w = end - k0
                    near = min(w, 2 * P)
                    bias = (w - near, 2 * P - near, near) if chunk == 0 else None
                    out.append(([(0, h, qb, k0, w, bias)], (w, h, qb, chunk)))
                    end, chunk = k0, chunk + 1
    else:
        for a in range(KB // 2):
            mms = [((h * 2 + i) * P, h, 2 * a + i, 0, SP, ((h * 2 + i) * P, i, SP) if a == 0 else None)
                   for h in range(2) for i in range(2)]
            out.append((mms, (S, None, 2 * a, 0)))
    rest = [m for m in out if m[1][2] >= KB // 2]
    out = out[:len(out) - len(rest)] + rest[:TURN_AFTER] + [TURN] + rest[TURN_AFTER:] + [TURN]
    assert len(out) % 2 == 0
    return out


def shares(units, first, last, total):
    room = [-bias for _, _, _, bias, _ in units]
    counts = [0] * len(units)
    for _ in range(total):
        u = max(range(first, last), key=lambda u: room[u])
        counts[u] += 1
        room[u] -= GW
    return counts


def attention(k, name, dr, ident, identr, causal, weights):
    nc = k.nc
    N = NPAIR * B
    nbuf, ahead = (2, 1) if causal else (4, 2)
    unroll = nbuf
    KR = P if causal else S
    NK = T if causal else SP
    NKB = KB if causal else 1
    units, msteps = units_of(causal), max_steps_of(causal)
    opens = [min(u for u in range(len(units)) if units[u][0] == g) for g in range(GB)]
    NU, NM = len(units), len(msteps)
    late = next((a for a, (mms, _) in enumerate(msteps) if mms and mms[0][2] >= KB // 2), None) if causal else None
    turns = [a for a in range(NM) if msteps[a] is TURN]
    last_of = [turns[0] - TURN_AFTER - 1, NM - 2]
    NCH = max(r[3] for _, r in msteps if r) + 1
    near = [u for u in range(NU) if units[u][3]]
    NB = len(near)
    ends = {max(u for u in range(NU) if units[u][0] == g): g for g in range(GB)}
    first, last = (4, NU) if causal else (0, NU)
    row_after = GB // 2 - 1
    NW = NM - 1
    counts = shares(units, first, last, NW)
    steps_at = {u: [(ahead, sum(counts[:u]) + i) for i in range(counts[u])] for u in range(first, last)}
    steps_at[0] = [(ahead - 1, NM - 1)] + steps_at.get(0, [])
    halves = [slice(0, T // 2), slice(T // 2, T)] if causal else [slice(0, T)]
    inits = 5 + nbuf * (1 if causal else 3)
    assert sum(len(r) for r in steps_at.values()) == NM
    with k:
        qs = [k.sb(f"{name}_q{i}", [QK, 2, T], F32R) for i in range(nbuf)]
        ks = [k.sb(f"{name}_k{i}", [QK, 2, NK], F32R) for i in range(nbuf)]
        vs = [k.sb(f"{name}_v{i}", [KR, NKB, 2, VW]) for i in range(nbuf)]
        tb = [k.sb(f"{name}_tb{i}", [KR, 2, 2 * P]) for i in range(nbuf)]
        ub = [k.sb(f"{name}_ub{i}", [P, 2, 2 * P] if causal else [P, 2, 2, SP], F32R) for i in range(nbuf)]
        pr = k.sb(f"{name}_pr", [KR, 2, 2, GW])
        part = k.sb(f"{name}_part", [P, 2, KB, NCH])
        rmax = k.sb(f"{name}_rmax", [P, 2, KB])
        neg = k.sb(f"{name}_neg", [KB, 2, P], F32R)
        osb = k.sb(f"{name}_osb", [P, 2, GW])
        st = [k.ps(f"{name}_st{i}", [P, 2, GW]) for i in range(2)]
        mp = [k.ps(f"{name}_mp{i}", [P, 512]) for i in range(2)]
        ov = [k.ps(f"{name}_ov{i}", [P, GW]) for i in range(2)]
        s = k.sems(name, "init in0 in1 in2 in3 rest0 rest1 scores bias exp av out st0 st1 chunk red max row0 row1")
        block = k.block()

        def place(n):
            return Step(n.t, n.i // B, n.unroll // B), n.i % B

        @block.sync
        def _(sp):
            def load(n):
                pair, b = place(n)
                waits(sp, s["av"], NU * n - (nbuf - 1) * NU + 1)
                to, done = n.par, s[f"in{n.par}"]
                q, kk = dr["qk"][0], dr["qk"][1] if causal else dr["ck"].ap()[b]
                rows = pair.cols(2 * HD)
                if causal:
                    heads = pair.cols(2)
                    sp.dma_start(raw(ub[to][:]), dr["sa_U"].ap()[heads].rearrange("h p j -> p h j")).then_inc(done, 16)
                for part_n, half in enumerate(halves):
                    if part_n:
                        done = s[f"rest{n.par}"]
                    tok = slice(b * T + half.start, b * T + half.stop)
                    keys, cols = (tok, half) if causal else (slice(0, S), slice(0, S))
                    for part_, hl in enumerate((0, 0, 1)):
                        sp.dma_start(raw(qs[to][part_ * HD:(part_ + 1) * HD, :, half]),
                                     q[hl, rows, tok].rearrange("(h d) t -> d h t", d=HD)).then_inc(done, 16)
                    for part_, hl in enumerate((0, 1, 0)):
                        sp.dma_start(raw(ks[to][part_ * HD:(part_ + 1) * HD, :, cols]),
                                     kk[hl, rows, keys].rearrange("(h d) t -> d h t", d=HD)).then_inc(done, 16)
                heads = pair.cols(2)
                if causal:
                    sp.dma_start(vs[to][:].rearrange("p k h e -> p k (h e)"),
                                 dr["v"][pair.cols(1), :, b * KB:(b + 1) * KB, :].rearrange("a p k e -> (a p) k e"))\
                      .then_inc(done, 16)
                    sp.dma_start(tb[to][:], dr["sa_T"].ap()[heads].rearrange("h p j -> p h j")).then_inc(done, 16)
                else:
                    sp.dma_start(vs[to][:].rearrange("p k h e -> p k (h e)"),
                                 dr["cv"].ap()[pair.cols(1), b:b + 1].rearrange("a k p e -> (a p) k e")).then_inc(done, 16)
                    sp.dma_start(tb[to][:], dr["ca_T"].ap()[heads].rearrange("h p j -> p h j")).then_inc(done, 16)
                    for i in range(2):
                        sp.dma_start(raw(ub[to][:, i, :, 0:S]), dr["ca_U"].ap()[heads][i].rearrange("(a p) j -> p a j", p=P))\
                          .then_inc(done, 16)

            def store(n, g):
                pair, b = place(n)
                sp.wait_ge(s["out"], GB * n + g + 2)
                for h in range(2):
                    sp.dma_start(dr["o"][pair.cols(2)][h, :, b * T + g * GW:b * T + (g + 1) * GW],
                                 osb[64 * h:64 * h + VW, g % 2, :]).then_inc(s[f"st{g % 2}"], 16)

            for n in range(nbuf - 1):
                load(Step(0, n, unroll, nbuf))

            def row(n, half):
                sp.wait_ge(s["red"], NM * n + turns[half] + 2)
                for h in range(2):
                    sp.dma_start(raw(qs[n.par][3 * HD:QK, h, half * T // 2:(half + 1) * T // 2]),
                                 raw(neg[h * KB // 2:(h + 1) * KB // 2, half])).then_inc(s[f"row{half}"], 16)

            for n in range(ahead):
                row(Step(0, n, unroll, nbuf), 0)
                if n < ahead - 1:
                    row(Step(0, n, unroll, nbuf), 1)

            def slot(n, left):
                if left >= nbuf - 1:
                    load(n + (nbuf - 1))
                if left >= ahead - 1:
                    row(n + (ahead - 1), 1)
                for g in range(GB):
                    store(n, g)
                    if g == row_after and left >= ahead:
                        row(n + ahead, 0)
            run(sp, N, slot, unroll, nbuf)
            for i in range(2):
                sp.wait_ge(s[f"st{i}"], 16 * N * GB)

        loads, rest = (7, 8) if causal else (10, 0)

        def landed(eng, n, name_, count):
            eng.wait_ge(s[f"{name_}{n.par}"], 16 * count * n.uses + 16 * count)

        @block.gpsimd
        def _(pool):
            if weights:
                pool.wait_ge(s["in0"], 16 * loads)
                weights.run(pool)

        @block.tensor
        def _(pe):
            for name_ in ("exp", "av", "out", "red"):
                pe.sem_inc(s[name_], 1)

            def max_step(n, a):
                if a == 0:
                    landed(pe, n, "in", loads)
                if a == late:
                    landed(pe, n, "rest", rest)
                mms, _ = msteps[a]
                waits(pe, s["red"], NM * n + a)
                out = mp[a % 2]
                if a in turns:
                    half = turns.index(a)
                    pe.wait_ge(s["max"], 2 * n + half + 1)
                    pe.transpose(out[0:KB, 0:P], rmax[:, half], ident[:]).then_inc(s["chunk"], 1)
                    return
                for c0, h, qb, k0, w, bias in mms:
                    last = pe.matmul(out[:, c0:c0 + w], qs[n.par][0:3 * HD, h, qb * P:(qb + 1) * P],
                                     ks[n.par][0:3 * HD, h, k0:k0 + w], start=True, stop=bias is None)
                    if bias:
                        b0, u0, bw = bias
                        rhs = ub[n.par][:, h, u0:u0 + bw] if causal else ub[n.par][:, h, u0, :]
                        last = pe.matmul(out[:, b0:b0 + bw], identr[:], rhs, start=False, stop=True)
                last.then_inc(s["chunk"], 1)

            def scores(n, u):
                g, kb, c0, _, _ = units[u]
                if u in (opens[0], opens[GB // 2]):
                    pe.wait_ge(s[f"row{g * 2 // GB}"], 32 * n + 32)
                waits(pe, s["exp"], NU * n + u)
                w = GW - c0
                for h in range(2):
                    last = pe.matmul(st[u % 2][0:KR, h, 0:w], ks[n.par][:, h, kb * P:kb * P + KR],
                                     qs[n.par][:, h, g * GW + c0:(g + 1) * GW], start=True, stop=True)
                last.then_inc(s["scores"], 1)

            def values(n, u):
                g, kb, c0, _, _ = units[u]
                if u in opens:
                    waits(pe, s["out"], GB * n + g)
                pe.wait_ge(s["exp"], NU * n + u + 2)
                stop = u in ends
                for h in range(2):
                    last = pe.matmul(ov[g % 2][64 * h:64 * h + VW, c0:GW], vs[n.par][:, kb, h, :],
                                     pr[:, u % 2, h, 0:GW - c0], start=(u in opens), stop=stop)
                last.then_inc(s["av"], 1)

            pe.wait_ge(s["init"], inits)
            for n in range(ahead):
                for a in range(NM - (n == ahead - 1)):
                    max_step(Step(0, n, unroll, nbuf), a)
            scores(Step(0, 0, unroll, nbuf), 0)

            def slot(n, left):
                for u in range(NU):
                    if u + 1 < NU:
                        scores(n, u + 1)
                    elif left:
                        scores(n + 1, 0)
                    steps = [(d, a) for d, a in steps_at.get(u, ()) if left >= d]
                    for d, a in steps[:1 if causal else 2]:
                        max_step(n + d, a)
                    values(n, u)
                    for d, a in steps[1 if causal else 2:]:
                        max_step(n + d, a)
            run(pe, N, slot, unroll, nbuf)

        @block.scalar
        def _(act):
            def empty(n, u):
                if u in ends:
                    g = ends[u]
                    act.wait_ge(s["av"], NU * n + u + 2)
                    waits(act, s[f"st{g % 2}"], (32 * GB // 2) * n + 32 * (g // 2))
                    act.activation(osb[:, g % 2, :], ov[g % 2][:], ACT.Copy).then_inc(s["out"], 1)

            def slot(n, left):
                for u in range(NU):
                    w = GW - units[u][2]
                    if u in near:
                        act.wait_ge(s["bias"], NB * n + near.index(u) + 1)
                    else:
                        act.wait_ge(s["scores"], NU * n + u + 1)
                    waits(act, s["av"], NU * n + u)
                    act.activation(pr[:, u % 2, :, 0:w], st[u % 2][0:KR, :, 0:w], ACT.Exp,
                                   scale=SCALE).then_inc(s["exp"], 1)
                    if u:
                        empty(n, u - 1)
                empty(n, NU - 1)
            run(act, N, slot, unroll, nbuf)

        @block.vector
        def _(dve):
            for t in ks:
                dve.memset(raw(t[3 * HD:QK]), 1.0).then_inc(s["init"], 1)
            dve.memset(part[:], NEG).then_inc(s["init"], 1)
            if not causal:
                for t, u_ in zip(ks, ub):
                    dve.memset(raw(t[0:3 * HD, :, S:SP]), 0.0).then_inc(s["init"], 1)
                    dve.memset(raw(u_[:, :, :, S:SP]), 0.0).then_inc(s["init"], 1)
            for t in ov:
                dve.memset(t[:], 0.0).then_inc(s["init"], 1)
            for t in mp:
                dve.memset(t[:], 0.0).then_inc(s["init"], 1)
            dve.wait_ge(s["init"], inits)

            def reduce(n, a):
                _, red = msteps[a]
                dve.wait_ge(s["chunk"], NM * n + a + 1)
                if a in turns:
                    half = turns.index(a)
                    waits(dve, s[f"row{half}"], 32 * n)
                    dve.tensor_scalar(neg[:, half], mp[a % 2][0:KB, 0:P], -1.0, None, ALU.mult).then_inc(s["red"], 1)
                    return
                w, h, qb, chunk = red
                if a == 0:
                    waits(dve, s["max"], 2 * n)
                if causal:
                    dve.tensor_reduce(part[:, h, qb, chunk:chunk + 1], mp[a % 2][:, 0:w], AX_X, ALU.max)\
                       .then_inc(s["red"], 1)
                else:
                    dve.tensor_reduce(part[:, :, qb:qb + 2, 0], mp[a % 2][:].rearrange("p (h i k) -> p h i k", h=2, i=2)[:, :, :, 0:w],
                                      AX_X, ALU.max).then_inc(s["red"], 1)
                if a in last_of:
                    half = last_of.index(a)
                    dve.wait_ge(s["red"], NM * n + a + 2)
                    dve.tensor_reduce(rmax[:, half].rearrange("p (h b) -> p h b", h=2),
                                      part[:, :, half * KB // 2:(half + 1) * KB // 2, :], AX_X, ALU.max)\
                       .then_inc(s["max"], 1)

            def bias(n, u):
                _, _, _, w, t0 = units[u]
                if w:
                    dve.wait_ge(s["scores"], NU * n + u + 1)
                    tile = st[u % 2][0:KR, :, 0:w]
                    dve.tensor_tensor(tile, tile, tb[n.par][:, :, t0:t0 + w], ALU.add).then_inc(s["bias"], 1)

            for n in range(ahead):
                for a in range(NM - (n == ahead - 1)):
                    reduce(Step(0, n, unroll, nbuf), a)
            bias(Step(0, 0, unroll, nbuf), 0)

            def slot(n, left):
                for u in range(NU):
                    if u + 1 < NU:
                        bias(n, u + 1)
                    elif left:
                        bias(n + 1, 0)
                    for d, a in steps_at.get(u, ()):
                        if left >= d:
                            reduce(n + d, a)
            run(dve, N, slot, unroll, nbuf)


def attention_out(k, name, io, dr, ident, w, src, dst, wq):
    nc = k.nc
    wo_h, wo_l = w
    with k:
        ot = k.sb(f"{name}o_ot", [P, 2, KC, GW])
        rb = k.sb(f"{name}o_rb", [P, 2, KC, GW])
        oh = k.sb(f"{name}o_oh", [P, 2, KC, GW], F32R)
        ol = k.sb(f"{name}o_ol", [P, 2, KC, GW], F32R)
        y = k.sb(f"{name}o_y", [P, 2, TT, D])
        sums = k.sb(f"{name}o_sums", [P, B * T * H // P])
        inv = k.sb(f"{name}o_inv", [P, B * T * H // P])
        brow = k.sb(f"{name}o_brow", [P, D])
        ops = [k.ps(f"{name}_ops{i}", [P, GW]) for i in range(4)]
        s = k.sems(f"{name}_out", "cols sums inv invst o0 o1 y0 y1 mul hi lo mm biased y st0 st1")
        if wq:
            lncols = k.sb(f"{name}o_lncols", [P, 2, KC])
            bcol = k.sb(f"{name}o_bcol", [P, KC])
            qst = k.sb(f"{name}o_qst", [P, KC, 2, GW], F32R)
            qps = [k.ps(f"{name}_qps{i}", [P, GW]) for i in range(2)]
            norm = Norm(k, f"{name}_ln", lncols, ident)
            sq = k.sems(f"{name}q", "mm hi ev held q0 q1 q2 q3")
        block = k.block()
        ncol = 48 if wq else 16

        @block.sync
        def _(sp):
            E = T * B // P * H
            sp.dma_start(sums[:],
                         dr["o"][:, HD, :].rearrange("h (e t) -> h e t", t=E)).then_inc(s["sums"], 16)

            def load_o(g):
                waits(sp, s["lo"], KC * g - KC)
                for j in range(HC):
                    sp.dma_start(ot[j * HD:(j + 1) * HD, g.par],
                                 dr["o"].rearrange("(c j) d t -> j d c t", j=HC)[j, 0:HD, :, g.cols(GW)]).then_inc(s[f"o{g.par}"], 16)

            def load_inv(g):
                for j in range(HC):
                    sp.dma_start(rb[j * HD:(j + 1) * HD, g.par],
                                 dr["inv"].ap().rearrange("(c j) t -> j c t", j=HC)[j, :, g.cols(GW)].partition_broadcast(HD))\
                      .then_inc(s[f"o{g.par}"], 16)

            def load_y(g):
                waits(sp, s[f"st{g.par}"], 16 * g.uses)
                if wq:
                    waits(sp, norm.s["normed"], TT * g - TT)
                sp.dma_start(y[:, g.par], src[:, g.cols(TT), :]).then_inc(s[f"y{g.par}"], 16)

            load_o(Step(0, 0))
            sp.dma_start(brow[:], io[f"{name}_bo"].partition_broadcast(P)).then_inc(s["cols"], 16)
            if wq:
                sp.dma_start(lncols[:], io["ln2"]).then_inc(s["cols"], 16)
                sp.dma_start(bcol[:], io["ca_bq"]).then_inc(s["cols"], 16)
            sp.wait_ge(s["inv"], 1)
            sp.dma_start(dr["inv"].ap().rearrange("h (e t) -> (h e) t", t=E), inv[:]).then_inc(s["invst"], 16)
            sp.wait_ge(s["invst"], 16)
            load_inv(Step(0, 0))
            load_y(Step(0, 0))
            load_o(Step(0, 1))
            load_inv(Step(0, 1))
            load_y(Step(0, 1))

            def store_y(g):
                sp.wait_ge(s["y"], TT * g + TT)
                sp.dma_start(dst[:, g.cols(TT), :], y[:, g.par]).then_inc(s[f"st{g.par}"], 16)

            load_o(Step(0, 2))
            load_inv(Step(0, 2))
            store_y(Step(0, 0))

            def slot(g, left):
                if left >= 3:
                    load_o(g + 3)
                    load_inv(g + 3)
                if left >= 1:
                    store_y(g + 1)
                if left >= 2:
                    load_y(g + 2)
                if wq:
                    for m in range(KC):
                        sp.wait_ge(sq["ev"], KC * g + m + 2)
                        sp.sem_inc(sq["held"], 1)
                        sp.dma_start(dr["qk"][0][:, m * P:(m + 1) * P, g.cols(GW)].rearrange("l p t -> p l t"),
                                     raw(qst[:, m])).then_inc(sq[f"q{m}"], 16)
            run(sp, NG, slot, tail=2)
            for i in range(2):
                sp.wait_ge(s[f"st{i}"], 16 * NG // 2)
            for m in range(KC if wq else 0):
                sp.wait_ge(sq[f"q{m}"], 16 * NG)

        @block.gpsimd
        def _(pool):
            pool.wait_ge(s["cols"], ncol)

            def slot(g, left):
                pool.wait_ge(s[f"y{g.par}"], 16 * g.uses + 16)
                for i in range(TT):
                    pool.tensor_tensor(y[:, g.par, i, :], y[:, g.par, i, :], brow[:], ALU.add).then_inc(s["biased"], 1)
            run(pool, NG, slot)

        @block.tensor
        def _(pe):
            if wq:
                norm.start(pe)
                pe.sem_inc(sq["ev"], 1)

            def project(g):
                waits(pe, s["y"], TT * g)
                for i in range(TT):
                    t = slice(i * P, (i + 1) * P)
                    if i == 0:
                        pe.wait_ge(s["lo"], KC * g + KC)
                    product(pe, ops[i][:], [((oh[:, g.par, c, t], ol[:, g.par, c, t]), (wo_h[:, c, :], wo_l[:, c, :]))
                                            for c in range(KC)]).then_inc(s["mm"], 1)

            project(Step(0, 0))
            if wq:
                norm.transpose(pe, Step(0, 0))

            def slot(g, left):
                if left:
                    project(g + 1)
                if wq:
                    norm.wait_ready(pe, g)
                    for m in range(KC):
                        waits(pe, sq["ev"], KC * g + m)
                        cols = slice(m * P, (m + 1) * P)
                        product(pe, qps[m % 2][:], [((wq[0][:, c, cols], wq[1][:, c, cols]), norm.pair(g.par, c))
                                                    for c in range(KC)]).then_inc(sq["mm"], 1)
                    if left:
                        norm.transpose(pe, g + 1)
            run(pe, NG, slot)

        @block.scalar
        def _(act):
            def high(g):
                for c in range(KC):
                    act.wait_ge(s["mul"], KC * g + c + 1)
                    if c == 0:
                        waits(act, s["mm"], TT * g - TT)
                    act.activation(oh[:, g.par, c, :], ot[:, g.par, c, :], ACT.Copy).then_inc(s["hi"], 1)

            high(Step(0, 0))
            high(Step(0, 1))
            act.wait_ge(s["cols"], ncol)
            if wq:
                norm.root(act, Step(0, 0))
                norm.scale(act, Step(0, 0), 0, (sq["mm"], 0))

            def slot(g, left):
                if left >= 2:
                    high(g + 2)
                if wq and left:
                    norm.root(act, g + 1)
                if wq:
                    for m in range(KC):
                        act.wait_ge(sq["mm"], KC * g + m + 1)
                        waits(act, sq[f"q{m}"], 16 * g)
                        act.activation(qst[:, m, 0, :], qps[m % 2][:], ACT.Identity,
                                       bias=bcol[:, m:m + 1]).then_inc(sq["hi"], 1)
                if wq and left:
                    norm.scale(act, g + 1, 1 - g.par, (sq["mm"], KC * g))
            run(act, NG, slot)

        @block.vector
        def _(dve):
            dve.wait_ge(s["sums"], 16)
            dve.reciprocal(inv[:], sums[:]).then_inc(s["inv"], 1)

            def multiply(g, c):
                if c == 0:
                    dve.wait_ge(s[f"o{g.par}"], 128 * g.uses + 128)
                dve.tensor_tensor(ot[:, g.par, c, :], ot[:, g.par, c, :], rb[:, g.par, c, :], ALU.mult)\
                   .then_inc(s["mul"], 1)

            def low(g, c):
                dve.wait_ge(s["hi"], KC * g + c + 1)
                dve.tensor_tensor(ol[:, g.par, c, :], ot[:, g.par, c, :], raw(oh[:, g.par, c, :]), ALU.subtract)\
                   .then_inc(s["lo"], 1)

            def residual(g, further):
                for i in range(TT):
                    if further:
                        multiply(g + 1, i)
                    dve.wait_ge(s["mm"], TT * g + i + 1)
                    dve.wait_ge(s["biased"], TT * g + i + 1)
                    dve.tensor_tensor(y[:, g.par, i, :], ops[i][:], y[:, g.par, i, :], ALU.add).then_inc(s["y"], 1)
                    if further and i:
                        low(g + 1, i - 1)
                    if wq:
                        dve.wait_ge(s["y"], TT * g + i + 1)
                        norm.stats(dve, y[:, g.par], i)
                if wq:
                    norm.normalise(dve, g, y[:, g.par], counted=True)
                if further:
                    low(g + 1, KC - 1)

            for c in range(KC):
                multiply(Step(0, 0), c)
            for c in range(KC):
                low(Step(0, 0), c)
            residual(Step(0, 0), True)
            dve.wait_ge(s["cols"], ncol)
            if wq:
                norm.low(dve, Step(0, 0), 0)

            def slot(g, left):
                if left:
                    residual(g + 1, left >= 2)
                if wq:
                    for m in range(KC):
                        dve.wait_ge(sq["hi"], KC * g + m + 1)
                        dve.scalar_tensor_tensor(qst[:, m, 1, :], qps[m % 2][:], bcol[:, m:m + 1],
                                                 raw(qst[:, m, 0, :]), ALU.add, ALU.subtract).then_inc(sq["ev"], 1)
                if wq and left:
                    norm.low(dve, g + 1, 1 - g.par)
            run(dve, NG, slot)


def feed_forward(k, io, dr, ident, w1, w2, W2, src):
    nc = k.nc
    with k:
        lncols = k.sb("ff_lncols", [P, 2, KC])
        b1 = k.sb("ff_b1", [P, FC])
        b2 = k.sb("ff_b2", [P, D])
        y = k.sb("ff_y", [P, 2, TT, D])
        hf = k.sb("ff_hf", [P, 2, GW])
        hh = k.sb("ff_hh", [P, 2, GW], F32R)
        hl = k.sb("ff_hl", [P, 2, GW], F32R)
        fps = [k.ps(f"ff_f{i}", [P, GW]) for i in range(2)]
        ops = [k.ps(f"ff_o{i}", [P, D]) for i in range(4)]
        norm = Norm(k, "ff_ln", lncols, ident)
        s = k.sems("ff", "cols y0 y1 mm relu hi lo used biased y st0 st1")
        block = k.block()

        @block.sync
        def _(sp):
            def load_y(g):
                waits(sp, s[f"st{g.par}"], 16 * g.uses)
                sp.dma_start(y[:, g.par], src[:, g.cols(TT), :]).then_inc(s[f"y{g.par}"], 16)

            load_y(Step(0, 0))
            sp.dma_start(lncols[:], io["ln3"]).then_inc(s["cols"], 16)
            sp.dma_start(b1[:], io["ff_b1"]).then_inc(s["cols"], 16)
            sp.dma_start(b2[:], io["ff_b2"].partition_broadcast(P)).then_inc(s["cols"], 16)

            def slot(g, left):
                if left:
                    load_y(g + 1)
                sp.wait_ge(s["y"], TT * g + TT)
                sp.dma_start(io["out"][:, g.cols(TT), :], y[:, g.par]).then_inc(s[f"st{g.par}"], 16)
            run(sp, NG, slot)
            for i in range(2):
                sp.wait_ge(s[f"st{i}"], 16 * NG // 2)

        @block.gpsimd
        def _(pool):
            W2.run(pool)
            pool.wait_ge(s["cols"], 48)

            def slot(g, left):
                pool.wait_ge(norm.s["normed"], TT * g + TT)
                for i in range(TT):
                    pool.tensor_tensor(y[:, g.par, i, :], y[:, g.par, i, :], b2[:], ALU.add).then_inc(s["biased"], 1)
            run(pool, NG, slot)

        @block.tensor
        def _(pe):
            norm.start(pe)
            for name in ("relu", "lo", "used"):
                pe.sem_inc(s[name], 1)

            def first(g, f):
                if f == 0:
                    norm.wait_ready(pe, g)
                waits(pe, s["relu"], FC * g + f)
                cols = slice(f * P, (f + 1) * P)
                product(pe, fps[f % 2][:], [((w1[0][:, c, cols], w1[1][:, c, cols]), norm.pair(g.par, c))
                                            for c in range(KC)]).then_inc(s["mm"], 1)

            def second(g, f):
                if f == 0:
                    waits(pe, s["y"], TT * g)
                pe.wait_ge(s["lo"], FC * g + f + 2)
                for i in range(TT):
                    t = slice(i * P, (i + 1) * P)
                    for n, (a, b) in enumerate(((hh, w2[0]), (hh, w2[1]), (hl, w2[0]))):
                        last = pe.matmul(ops[i][:], a[:, f % 2, t], b[:, f, :],
                                         start=(f == 0 and n == 0), stop=(f == FC - 1 and n == 2))
                last.then_inc(s["used"], 1)

            norm.transpose(pe, Step(0, 0))
            first(Step(0, 0), 0)

            def slot(g, left):
                for f in range(FC):
                    if f + 1 < FC:
                        first(g, f + 1)
                    elif left:
                        first(g + 1, 0)
                    if f == 9 and left:
                        norm.transpose(pe, g + 1)
                    if isinstance(g.n, int) and g.n == 0:
                        pe.wait_ge(W2.s["lo"], 2 * f + 2)
                    second(g, f)
            run(pe, NG, slot)

        @block.scalar
        def _(act):
            act.wait_ge(s["cols"], 48)
            norm.root(act, Step(0, 0))
            norm.scale(act, Step(0, 0), 0, (s["mm"], 0))

            def slot(g, left):
                for f in range(FC):
                    if f == 5 and left:
                        norm.root(act, g + 1)
                    if f == 10 and left:
                        norm.scale(act, g + 1, 1 - g.par, (s["mm"], FC * g))
                    act.wait_ge(s["mm"], FC * g + f + 1)
                    waits(act, s["lo"], FC * g + f)
                    act.activation(hf[:, f % 2, :], fps[f % 2][:], ACT.Relu, bias=b1[:, f:f + 1]).then_inc(s["relu"], 1)
                    act.wait_ge(s["relu"], FC * g + f + 2)
                    waits(act, s["used"], FC * g + f)
                    act.activation(hh[:, f % 2, :], hf[:, f % 2, :], ACT.Copy).then_inc(s["hi"], 1)
            run(act, NG, slot)

        @block.vector
        def _(dve):
            dve.wait_ge(s["cols"], 48)
            dve.wait_ge(s["y0"], 16)
            norm.normalise(dve, Step(0, 0), y[:, 0])
            norm.low(dve, Step(0, 0), 0)

            def slot(g, left):
                for f in range(FC):
                    if f == 5 and left:
                        dve.wait_ge(s[f"y{1 - g.par}"], 16 * (g + 1).uses + 16)
                        norm.normalise(dve, g + 1, y[:, 1 - g.par])
                    if f == 10 and left:
                        norm.low(dve, g + 1, 1 - g.par)
                    dve.wait_ge(s["hi"], FC * g + f + 1)
                    dve.tensor_tensor(hl[:, f % 2, :], hf[:, f % 2, :], raw(hh[:, f % 2, :]), ALU.subtract)\
                       .then_inc(s["lo"], 1)
                dve.wait_ge(s["used"], FC * g + FC + 1)
                for i in range(TT):
                    dve.wait_ge(s["biased"], TT * g + i + 1)
                    dve.tensor_tensor(y[:, g.par, i, :], ops[i][:], y[:, g.par, i, :], ALU.add).then_inc(s["y"], 1)
            run(dve, NG, slot)


def transformer(nc, io):
    k = Core(nc)
    scratch = lambda name, shape: nc.dram_tensor(f"scratch_{name}", shape, F32, kind="Internal")
    q, kk = scratch("q", (2, D, TOK)), scratch("k", (2, D, TOK))
    y1, y2 = scratch("y1", (P, NG * TT, D)), scratch("y2", (P, NG * TT, D))
    o = scratch("o", (H, VW, TOK))
    dr = {
        "rows": scratch("rows", (H, 5, GL)), "en_B": scratch("en_B", (H, S, S)),
        "sa_T": scratch("sa_T", (H, P, 2 * P)), "sa_U": scratch("sa_U", (H, P, 2 * P)),
        "ca_T": scratch("ca_T", (H, S, 2 * P)), "ca_U": scratch("ca_U", (H, 2 * P, S)),
        "ck": scratch("ck", (B, 2, D, S)), "cv": scratch("cv", (NPAIR, B, S, 2 * VW)),
        "qk": (q.ap(), kk.ap()), "v": scratch("v", (NPAIR, P, B * KB, 2 * VW)).ap(),
        "o": o.ap(), "inv": scratch("inv", (H, TOK)),
    }
    with k:
        ident = k.sb("ident", [P, P])
        identr = k.sb("identr", [P, P], F32R)
        with k:
            wqkv = [k.sb(f"qkv_w{i}", [P, KC, 3 * D], F32R) for i in range(2)]
            with k:
                part = 3 * D // 4
                split = SplitWeights(k, "qkv_w", [(io["sa_wqkv"][:, c, f:f + part], wqkv[0][:, c, f:f + part],
                                                   wqkv[1][:, c, f:f + part]) for c in range(KC) for f in range(0, 3 * D, part)], part)
                encoder(k, io, dr, ident, identr, split)
            decoder_qkv(k, io, dr, ident, wqkv)
        with k:
            wo = [k.sb(f"sa_wo{i}", [P, KC, D], F32R) for i in range(2)]
            wq = [k.sb(f"ca_wq{i}", [P, KC, D], F32R) for i in range(2)]
            split = SplitWeights(k, "out_w", [(io[n][:, c], w[0][:, c, :], w[1][:, c, :])
                                              for n, w in (("sa_wo", wo), ("ca_wq", wq)) for c in range(KC)], D)
            attention(k, "sa", dr, ident, identr, True, split)
            attention_out(k, "sa", io, dr, ident, wo, io["x"], y1.ap(), wq)
        with k:
            w1 = [k.sb(f"ff_w1_{i}", [P, KC, DFF], F32R) for i in range(2)]
            with k:
                wo = [k.sb(f"ca_wo{i}", [P, KC, D], F32R) for i in range(2)]
                jobs = [(io["ca_wo"][:, c], wo[0][:, c, :], wo[1][:, c, :]) for c in range(KC)]
                for c in range(KC):
                    for f in range(0, DFF, D):
                        jobs.append((io["ff_w1"][:, c, f:f + D], w1[0][:, c, f:f + D], w1[1][:, c, f:f + D]))
                split = SplitWeights(k, "ca_w", jobs, D)
                attention(k, "ca", dr, ident, identr, False, split)
                attention_out(k, "ca", io, dr, ident, wo, y1.ap(), y2.ap(), None)
            with k:
                w2 = [k.sb(f"ff_w2_{i}", [P, FC, D], F32R) for i in range(2)]
                jobs = [(io["ff_w2"][:, f, h:h + D // 2], w2[0][:, f, h:h + D // 2], w2[1][:, f, h:h + D // 2])
                        for f in range(FC) for h in range(0, D, D // 2)]
                split = SplitWeights(k, "ff_w", jobs, D // 2)
                feed_forward(k, io, dr, ident, w1, w2, split, y2.ap())


def kernel(**inputs):
    import numpy as np
    import concourse.bacc as bacc
    from concourse.bass_utils import run_bass_kernel_spmd as launch

    a = {n.removeprefix("L0_xattn_"): np.asarray(v) for n, v in inputs.items()}

    def contraction_major(w):
        return w.T.reshape(-1, P, w.shape[0]).transpose(1, 0, 2)

    def column(v):
        return v.reshape(-1, P).T

    def tokens(v):
        return v.reshape(-1, P, D).transpose(1, 0, 2)

    def bucket(r):
        return np.where(r < 0, np.minimum(-r, P - 1), np.minimum(r, P - 1) + P)

    far = 2 * P
    sa, ca, en = np.arange(1 - P, far), np.arange(1 - S, far), np.arange(1 - S, S)
    rel = np.zeros((H, 5, GL), np.float32)
    for i, (table, r) in enumerate((("dec_rel_self", -sa), ("dec_rel_self", -sa[::-1]), ("dec_rel_cross", -ca),
                                    ("dec_rel_cross", -ca[::-1]), ("enc_rel", en))):
        rel[:, i, :len(r)] = a[table][bucket(r)].T

    ca_b = a["dec_ca_in_b"]
    arrays = {
        "x": tokens(a["x"]),
        "ctxT": a["ctx_1024"].reshape(SE, D).T.reshape(KC, P, SE).transpose(1, 0, 2),
        "enc_wqkv": contraction_major(a["enc_in_w"]),
        "enc_wo": contraction_major(a["enc_out_w"]),
        "enc_wff1": contraction_major(a["enc_ff1_w"]),
        "enc_wff2": contraction_major(a["enc_ff2_w"]),
        "enc_wkv": contraction_major(a["dec_ca_in_w"][D:]),
        "enc_cols": np.concatenate([column(v) for v in (
            a["enc_n1_s"], a["enc_n1_b"], a["enc_n2_s"], a["enc_n2_b"], a["enc_in_b"][:2 * D], a["enc_out_b"],
            a["enc_ff1_b"], a["enc_ff2_b"], ca_b[D:2 * D])], axis=1),
        "enc_vrow": np.stack([a["enc_in_b"][2 * D:], ca_b[2 * D:]]),
        "rel_rows": rel,
        "sa_wqkv": contraction_major(a["dec_sa_in_w"]),
        "sa_bqk": column(a["dec_sa_in_b"][:2 * D]),
        "sa_bv": a["dec_sa_in_b"][2 * D:],
        "sa_wo": contraction_major(a["dec_sa_out_w"]),
        "sa_bo": a["dec_sa_out_b"],
        "ca_wq": contraction_major(a["dec_ca_in_w"][:D]),
        "ca_bq": column(ca_b[:D]),
        "ca_wo": contraction_major(a["dec_ca_out_w"]),
        "ca_bo": a["dec_ca_out_b"],
        "ff_w1": contraction_major(a["dec_ff1_w"]),
        "ff_b1": column(a["dec_ff1_b"]),
        "ff_w2": contraction_major(a["dec_ff2_w"]),
        "ff_b2": a["dec_ff2_b"],
    }
    for i in (1, 2, 3):
        arrays[f"ln{i}"] = np.stack([column(a[f"dec_n{i}_s"]), column(a[f"dec_n{i}_b"])], axis=1)

    nc = bacc.Bacc("TRN2", target_bir_lowering=False, num_devices=1)
    arrays = {n: np.ascontiguousarray(v) for n, v in arrays.items()}
    io = {n: nc.dram_tensor(f"in_{n}", v.shape, mybir.dt.from_np(v.dtype), kind="ExternalInput").ap()
          for n, v in arrays.items()}
    io["out"] = nc.dram_tensor("out_y", (P, NG * TT, D), F32, kind="ExternalOutput").ap()
    transformer(nc, io)
    r = launch(nc, [{f"in_{n}": v for n, v in arrays.items()}], core_ids=[0])
    return r.results[0]["out_y"].transpose(1, 0, 2).reshape(B, T, D)
```
